# Optimizing a Trainium2 kernel written in Bass

```python
import numpy as np
import jax
import jax.numpy as jnp

def _softmax(x, axis=-1):
    return jax.nn.softmax(x, axis=axis)

def _gelu(x):
    return jax.nn.gelu(x, approximate=True)

def _silu(x):
    return jax.nn.silu(x)

def _sigmoid(x):
    return jax.nn.sigmoid(x)

def _layernorm(x, axis=-1, eps=1e-05):
    m = jnp.mean(x, axis=axis, keepdims=True)
    v = jnp.var(x, axis=axis, keepdims=True)
    return (x - m) / jnp.sqrt(v + eps)

def _scatter_add(tgt, idx, src, axis=0):
    return tgt.at[idx].add(src)

def _segment_sum(src, seg, n):
    return jax.ops.segment_sum(src, seg, n)
kernel_name = 'mk_dlrm_tower_d1_rec_r8_547c8e'

def setup_inputs(seed: int=0):
    np.random.seed(seed)
    _w = jnp.asarray

    def _rec_inputs():
        import jax
        import jax.numpy as jnp
        _tk = jax.random.key(seed)
        ids = jnp.stack([jax.random.randint(jax.random.fold_in(_tk, 200 + f), (512,), 0, v, jnp.int32) for f, v in enumerate([125000, 1000, 1000, 12500, 1000, 12500, 12500, 12500, 1250, 12500, 12500, 12500, 1250, 1250, 12500, 1250, 1000, 1000, 1000, 1250, 1000, 1000, 1250, 1250, 1000, 1000])], axis=1)
        tbl_0 = 0.05 * jax.random.normal(jax.random.fold_in(_tk, 500 + 0), (125000, 128), jnp.float32)
        tbl_1 = 0.05 * jax.random.normal(jax.random.fold_in(_tk, 500 + 1), (1000, 128), jnp.float32)
        tbl_2 = 0.05 * jax.random.normal(jax.random.fold_in(_tk, 500 + 2), (1000, 128), jnp.float32)
        tbl_3 = 0.05 * jax.random.normal(jax.random.fold_in(_tk, 500 + 3), (12500, 128), jnp.float32)
        tbl_4 = 0.05 * jax.random.normal(jax.random.fold_in(_tk, 500 + 4), (1000, 128), jnp.float32)
        tbl_5 = 0.05 * jax.random.normal(jax.random.fold_in(_tk, 500 + 5), (12500, 128), jnp.float32)
        tbl_6 = 0.05 * jax.random.normal(jax.random.fold_in(_tk, 500 + 6), (12500, 128), jnp.float32)
        tbl_7 = 0.05 * jax.random.normal(jax.random.fold_in(_tk, 500 + 7), (12500, 128), jnp.float32)
        tbl_8 = 0.05 * jax.random.normal(jax.random.fold_in(_tk, 500 + 8), (1250, 128), jnp.float32)
        tbl_9 = 0.05 * jax.random.normal(jax.random.fold_in(_tk, 500 + 9), (12500, 128), jnp.float32)
        tbl_10 = 0.05 * jax.random.normal(jax.random.fold_in(_tk, 500 + 10), (12500, 128), jnp.float32)
        tbl_11 = 0.05 * jax.random.normal(jax.random.fold_in(_tk, 500 + 11), (12500, 128), jnp.float32)
        tbl_12 = 0.05 * jax.random.normal(jax.random.fold_in(_tk, 500 + 12), (1250, 128), jnp.float32)
        tbl_13 = 0.05 * jax.random.normal(jax.random.fold_in(_tk, 500 + 13), (1250, 128), jnp.float32)
        tbl_14 = 0.05 * jax.random.normal(jax.random.fold_in(_tk, 500 + 14), (12500, 128), jnp.float32)
        tbl_15 = 0.05 * jax.random.normal(jax.random.fold_in(_tk, 500 + 15), (1250, 128), jnp.float32)
        tbl_16 = 0.05 * jax.random.normal(jax.random.fold_in(_tk, 500 + 16), (1000, 128), jnp.float32)
        tbl_17 = 0.05 * jax.random.normal(jax.random.fold_in(_tk, 500 + 17), (1000, 128), jnp.float32)
        tbl_18 = 0.05 * jax.random.normal(jax.random.fold_in(_tk, 500 + 18), (1000, 128), jnp.float32)
        tbl_19 = 0.05 * jax.random.normal(jax.random.fold_in(_tk, 500 + 19), (1250, 128), jnp.float32)
        tbl_20 = 0.05 * jax.random.normal(jax.random.fold_in(_tk, 500 + 20), (1000, 128), jnp.float32)
        tbl_21 = 0.05 * jax.random.normal(jax.random.fold_in(_tk, 500 + 21), (1000, 128), jnp.float32)
        tbl_22 = 0.05 * jax.random.normal(jax.random.fold_in(_tk, 500 + 22), (1250, 128), jnp.float32)
        tbl_23 = 0.05 * jax.random.normal(jax.random.fold_in(_tk, 500 + 23), (1250, 128), jnp.float32)
        tbl_24 = 0.05 * jax.random.normal(jax.random.fold_in(_tk, 500 + 24), (1000, 128), jnp.float32)
        tbl_25 = 0.05 * jax.random.normal(jax.random.fold_in(_tk, 500 + 25), (1000, 128), jnp.float32)
        _rk = jax.random.fold_in(_tk, 7)
        r_bottom_output = -0.000520686 + 1.00062 * jax.random.normal(jax.random.fold_in(_rk, 101), (512, 128), jnp.float32)
        W_top1 = 0.0456912 * jax.random.normal(jax.random.fold_in(_tk, 801), (479, 512), jnp.float32)
        W_top2 = 0.0441942 * jax.random.normal(jax.random.fold_in(_tk, 802), (512, 256), jnp.float32)
        W_top3 = 0.0625 * jax.random.normal(jax.random.fold_in(_tk, 803), (256, 1), jnp.float32)
        b_top1 = jnp.zeros((512,), jnp.float32)
        b_top2 = jnp.zeros((256,), jnp.float32)
        return (r_bottom_output, ids, tbl_0, tbl_1, tbl_2, tbl_3, tbl_4, tbl_5, tbl_6, tbl_7, tbl_8, tbl_9, tbl_10, tbl_11, tbl_12, tbl_13, tbl_14, tbl_15, tbl_16, tbl_17, tbl_18, tbl_19, tbl_20, tbl_21, tbl_22, tbl_23, tbl_24, tbl_25, W_top1, b_top1, W_top2, b_top2, W_top3)
    r_bottom_output, ids, tbl_0, tbl_1, tbl_2, tbl_3, tbl_4, tbl_5, tbl_6, tbl_7, tbl_8, tbl_9, tbl_10, tbl_11, tbl_12, tbl_13, tbl_14, tbl_15, tbl_16, tbl_17, tbl_18, tbl_19, tbl_20, tbl_21, tbl_22, tbl_23, tbl_24, tbl_25, W_top1, b_top1, W_top2, b_top2, W_top3 = _rec_inputs()

    def _L0_rec_setup():
        import jax, jax.numpy as jnp
        import numpy as np
        NUM_FEATURES = 27
        _TRIU_I, _TRIU_J = np.triu_indices(NUM_FEATURES, k=1)
        key = jax.random.key(seed)
        k1, k2 = jax.random.split(key)
        bottom_output = jax.random.normal(k1, (2048, 128), dtype=jnp.float32)
        embeddings = jax.random.normal(k2, (2048, 26, 128), dtype=jnp.float32)
        return {'bottom_output': bottom_output, 'embeddings': embeddings}
    _L0_rec_all = _L0_rec_setup()
    _L0_rec_in = {k: v for k, v in _L0_rec_all.items() if k in ()}
    del _L0_rec_all
    return {'r_bottom_output': r_bottom_output, 'ids': ids, 'tbl_0': tbl_0, 'tbl_1': tbl_1, 'tbl_2': tbl_2, 'tbl_3': tbl_3, 'tbl_4': tbl_4, 'tbl_5': tbl_5, 'tbl_6': tbl_6, 'tbl_7': tbl_7, 'tbl_8': tbl_8, 'tbl_9': tbl_9, 'tbl_10': tbl_10, 'tbl_11': tbl_11, 'tbl_12': tbl_12, 'tbl_13': tbl_13, 'tbl_14': tbl_14, 'tbl_15': tbl_15, 'tbl_16': tbl_16, 'tbl_17': tbl_17, 'tbl_18': tbl_18, 'tbl_19': tbl_19, 'tbl_20': tbl_20, 'tbl_21': tbl_21, 'tbl_22': tbl_22, 'tbl_23': tbl_23, 'tbl_24': tbl_24, 'tbl_25': tbl_25, 'W_top1': W_top1, 'b_top1': b_top1, 'W_top2': W_top2, 'b_top2': b_top2, 'W_top3': W_top3}

def reference(r_bottom_output, ids, tbl_0, tbl_1, tbl_2, tbl_3, tbl_4, tbl_5, tbl_6, tbl_7, tbl_8, tbl_9, tbl_10, tbl_11, tbl_12, tbl_13, tbl_14, tbl_15, tbl_16, tbl_17, tbl_18, tbl_19, tbl_20, tbl_21, tbl_22, tbl_23, tbl_24, tbl_25, W_top1, b_top1, W_top2, b_top2, W_top3):
    import jax
    import jax.numpy as jnp

    def _L0_rec_ref(bottom_output, embeddings):
        import jax, jax.numpy as jnp
        import numpy as np
        NUM_FEATURES = 27
        _TRIU_I, _TRIU_J = np.triu_indices(NUM_FEATURES, k=1)
        all_emb = jnp.concatenate([bottom_output[:, None, :], embeddings], axis=1)
        gram = jnp.einsum('bfd,bgd->bfg', all_emb, all_emb)
        return gram[:, _TRIU_I, _TRIU_J]
    e = jnp.stack([tbl_0[ids[:, 0]], tbl_1[ids[:, 1]], tbl_2[ids[:, 2]], tbl_3[ids[:, 3]], tbl_4[ids[:, 4]], tbl_5[ids[:, 5]], tbl_6[ids[:, 6]], tbl_7[ids[:, 7]], tbl_8[ids[:, 8]], tbl_9[ids[:, 9]], tbl_10[ids[:, 10]], tbl_11[ids[:, 11]], tbl_12[ids[:, 12]], tbl_13[ids[:, 13]], tbl_14[ids[:, 14]], tbl_15[ids[:, 15]], tbl_16[ids[:, 16]], tbl_17[ids[:, 17]], tbl_18[ids[:, 18]], tbl_19[ids[:, 19]], tbl_20[ids[:, 20]], tbl_21[ids[:, 21]], tbl_22[ids[:, 22]], tbl_23[ids[:, 23]], tbl_24[ids[:, 24]], tbl_25[ids[:, 25]]], axis=1)
    z = _L0_rec_ref(r_bottom_output, e)
    z = z.reshape(z.shape[0], -1)
    h = jnp.concatenate([z, r_bottom_output], axis=1)
    h = jnp.maximum(h @ W_top1 + b_top1, 0.0)
    h = jnp.maximum(h @ W_top2 + b_top2, 0.0)
    y = h @ W_top3
    return y

_drawn_inputs = setup_inputs


def setup_inputs(seed=0):
    import zlib

    import numpy as np

    out = dict(_drawn_inputs(seed))
    spreads = {'b_top1': (0.0, 0.1), 'b_top2': (0.0, 0.1)}
    factors = {}
    for name, (base, spread) in spreads.items():
        noise = np.random.default_rng([zlib.crc32(name.encode()), seed]).standard_normal(out[name].shape)
        drawn = base * np.exp(spread * noise) if base else spread * noise
        out[name] = jnp.asarray(drawn.astype(out[name].dtype))
    for name, factor in factors.items():
        out[name] = (out[name] * factor).astype(out[name].dtype)
    return out
```

```python
from contextlib import ExitStack

import concourse.bass as bass
from concourse import mybir

F32 = mybir.dt.float32
F32R = mybir.dt.float32r
I32 = mybir.dt.int32
ALU = mybir.AluOpType
ACT = mybir.ActivationFunctionType

B = 512
D = 128
TABLES = 26
NF = TABLES + 1
LANES = 128
TILES = B // LANES
Q = 4
QP = 32
U = LANES // Q
LOOKED_UP = [1, 2, 4, 16, 17, 18, 20, 21]
GATHERED = [i for i in range(TABLES) if i not in LOOKED_UP]
SLOTS = [0] + [i + 1 for i in GATHERED] + [i + 1 for i in LOOKED_UP]
NG = len(GATHERED)
NL = len(LOOKED_UP)
TURNED = NG + 1
GROUP = 4
GROUPS = [range(a, min(a + GROUP, TURNED)) for a in range(0, TURNED, GROUP)]
ROWS = 1000
KP = 125
KC = ROWS // KP
HALF = KC // 2
DELTAS = NF // 2
ZG = 9
ZC = NF // ZG
ZK = ZG * DELTAS
H1, H2 = 512, 256
M1, M2 = H1 // 128, H2 // 128
UNIT = 8
UNITS = U // UNIT
BANKS = 4
OH_RING, HL_RING, RAW_RING = 3, 2, 2

ORDER = [("look", j) for j in range(NL)]
for _t in range(TILES - 1):
    ORDER += [("turn", _t)]
    if _t:
        ORDER += [("pairs", _t - 1), ("l1", _t - 1)]
    ORDER += [("gram", _t)]
    if _t:
        ORDER += [("l2", _t - 1), ("l3", _t - 1)]
_t = TILES - 1
ORDER += [("pairs", _t - 1), ("l1", _t - 1), ("l2", _t - 1), ("l3", _t - 1), ("turn", _t), ("gram", _t),
          ("pairs", _t), ("l1", _t), ("l2", _t), ("l3", _t)]

TAKES = {"look": 1, "turn": len(GROUPS), "pairs": 1, "l1": 2, "l2": 2, "l3": 1}
USES = [(step, i, part) for step, i in ORDER for part in range(TAKES.get(step, 0))]


def bank(step, i, part=0):
    return USES.index((step, i, part)) % BANKS


def by_act(g):
    return g % 2 == 0


ACT_GROUPS = sum(by_act(g) for g in range(len(GROUPS)))
DVE_GROUPS = len(GROUPS) - ACT_GROUPS


def tower(nc, bottom, ids, ids_t, tables, w1, b1, w2, b2, w3, out):
    ctx = ExitStack()
    with ctx:
        def sb(name, shape, dt=F32):
            return ctx.enter_context(nc.sbuf_tensor(name, shape, dt))

        def sem(name):
            return ctx.enter_context(nc.semaphore(name))

        ids_sb = sb("ids_sb", [128, TILES * TABLES], I32)
        bot = sb("bot", [128, TILES, D])
        rows = sb("rows", [128, TILES, NG, D])
        emb = sb("emb", [128, TILES, LANES, QP])
        gram = sb("gram", [128, 2, NF, U])
        pairs = sb("pairs", [128, NF - 1 + DELTAS, QP])
        z = sb("z", [128, NF * DELTAS])
        zt = sb("zt", [ZK, 2, ZC, LANES])
        h1 = sb("h1", [128, 2, M1, LANES])
        h2 = sb("h2", [128, 2, M2, LANES])
        y = sb("y", [1, B])
        raw = sb("raw", [KP, RAW_RING, KC * D])
        hi = sb("hi", [KP, HL_RING, KC * D], F32R)
        lo = sb("lo", [KP, HL_RING, KC * D], F32R)
        ids_b = sb("ids_b", [KP, NL, B], I32)
        onehot = sb("onehot", [KP, OH_RING, HALF, B], F32R)
        row_i = sb("row_i", [KP, KC], I32)
        row_f = sb("row_f", [KP, KC])
        ident = sb("ident", [128, 128])
        w1z = sb("w1z", [ZK, ZC, H1])
        w1b = sb("w1b", [128, H1])
        w2_sb = sb("w2_sb", [128, M1, H2])
        w3_sb = sb("w3_sb", [128, M2])
        b1_sb = sb("b1_sb", [128, M1])
        b2_sb = sb("b2_sb", [128, M2])

        ring = ctx.enter_context(nc.psum_tensor("ring", [128, BANKS, 512], F32))
        gps = ctx.enter_context(nc.psum_tensor("gps", [128, 2, UNIT, 128], F32))

        ids_in = sem("ids_in")
        bot_in = sem("bot_in")
        w_in = sem("w_in")
        raw_in = [sem(f"raw_in{k}") for k in range(RAW_RING)]
        idb_in = [sem(f"idb_in{j}") for j in range(NL)]
        rows_in = [[sem(f"rows_in{t}_{g}") for g in range(len(GROUPS))] for t in range(TILES)]
        out_done = sem("out_done")
        ident_set = sem("ident_set")
        pad_set = sem("pad_set")
        row_set = sem("row_set")
        row_ready = sem("row_ready")
        hi_ready = sem("hi_ready")
        lo_ready = sem("lo_ready")
        oh_ready = sem("oh_ready")
        oh_used = sem("oh_used")
        turned = sem("turned")
        emb_look = sem("emb_look")
        emb_act = sem("emb_act")
        emb_dve = sem("emb_dve")
        gram_done = sem("gram_done")
        cut_act = sem("cut_act")
        cut_dve = sem("cut_dve")
        pairs_ready = sem("pairs_ready")
        z_ready = sem("z_ready")
        pairs_done = sem("pairs_done")
        zt_ready = sem("zt_ready")
        l1_done = sem("l1_done")
        h1_act = sem("h1_act")
        h1_dve = sem("h1_dve")
        l2_done = sem("l2_done")
        h2_act = sem("h2_act")
        h2_dve = sem("h2_dve")
        l3_done = sem("l3_done")
        y_ready = sem("y_ready")

        def emb_slots(t, first, count):
            return emb[:, t, :, first:first + count].rearrange("d p f -> d f p")

        block = ctx.enter_context(nc.Block())

        @block.sync
        def _(sp):
            sp.dma_start(ids_sb[:], ids.rearrange("(p t) f -> p (t f)", t=TILES)).then_inc(ids_in, 16)
            for j in range(NL):
                if j >= RAW_RING:
                    sp.wait_ge(lo_ready, j - RAW_RING + 1)
                sp.dma_start(raw[:, j % RAW_RING, :],
                             tables[LOOKED_UP[j]].rearrange("(p k) d -> p (k d)", k=KC)
                             ).then_inc(raw_in[j % RAW_RING], 16)
                if j == RAW_RING - 1:
                    sp.dma_start(bot[:], bottom.rearrange("(p t) d -> p t d", t=TILES)).then_inc(bot_in, 16)
                    sp.dma_start(w1z[:], w1[0:ZC * ZK, :].rearrange("(c k) n -> k c n", c=ZC)).then_inc(w_in, 16)
                    sp.dma_start(w1b[:], w1[ZC * ZK:, :]).then_inc(w_in, 16)
                    sp.dma_start(w2_sb[:], w2.rearrange("(c k) n -> k c n", c=M1)).then_inc(w_in, 16)
                    sp.dma_start(w3_sb[:], w3).then_inc(w_in, 16)
                    sp.dma_start(b1_sb[:], b1).then_inc(w_in, 16)
                    sp.dma_start(b2_sb[:], b2).then_inc(w_in, 16)
            sp.wait_ge(y_ready, TILES)
            sp.dma_start(out.rearrange("b o -> o b"), y[:]).then_inc(out_done, 16)
            sp.wait_ge(out_done, 16)

        @block.gpsimd
        def _(pool):
            nc.gpsimd.iota(row_i[:], pattern=[[1, KC]], base=0, channel_multiplier=KC).then_inc(row_set, 1)
            pool.wait_ge(ids_in, 16)

            def gather(t, g):
                for slot in GROUPS[g]:
                    if slot == 0:
                        continue
                    table = GATHERED[slot - 1]
                    col = t * TABLES + table
                    nc.gpsimd.indirect_dma_start(
                        out=rows[:, t, slot - 1, :], out_offset=None, in_=tables[table],
                        in_offset=bass.IndirectOffsetOnAxis(ap=ids_sb[:, col:col + 1], axis=0),
                    ).then_inc(rows_in[t][g], 16)

            for t in range(TILES):
                for g in range(len(GROUPS)):
                    gather(t, g)
                if t == 0:
                    pool.wait_ge(pad_set, 1)
                    nc.gpsimd.affine_select(out=ident[:], in_=ident[:], compare_op=ALU.is_equal, fill=0.0,
                                            base=0, pattern=[[-1, 128]],
                                            channel_multiplier=1).then_inc(ident_set, 1)

        @block.scalar
        def _(act):
            for j in range(NL):
                row = ids_t[LOOKED_UP[j]:LOOKED_UP[j] + 1, :]
                act.dma_start(ids_b[:, j, :], row.broadcast_to([KP, B])).then_inc(idb_in[j], 16)

            def split(j):
                act.wait_ge(raw_in[j % RAW_RING], 16 * (j // RAW_RING + 1))
                if j >= HL_RING:
                    act.wait_ge(oh_used, 2 * (j - HL_RING + 1))
                nc.scalar.copy(hi[:, j % HL_RING, :], raw[:, j % RAW_RING, :]).then_inc(hi_ready, 1)

            for step, t in ORDER:
                if step == "look":
                    if t == 0:
                        split(0)
                    if t + 1 < NL:
                        split(t + 1)
                    act.wait_ge(oh_used, 2 * (t + 1))
                    b = bank(step, t)
                    slot = TURNED + t
                    nc.scalar.copy(emb[:, :, :, slot], ring[:, b, :].rearrange("d (p t) -> d t p", t=TILES)
                                   ).then_inc(emb_look, 1)
                elif step == "turn":
                    for g, slots in enumerate(GROUPS):
                        if not by_act(g):
                            continue
                        act.wait_ge(turned, t * len(GROUPS) + g + 1)
                        b = bank(step, t, g)
                        n = len(slots)
                        nc.scalar.copy(emb_slots(t, slots[0], n),
                                       ring[:, b, 0:n * LANES].rearrange("d (f p) -> d f p", f=n)
                                       ).then_inc(emb_act, 1)
                elif step == "gram":
                    if t >= 2:
                        act.wait_ge(pairs_ready, 2 * (t - 1))
                    for n in range(UNITS):
                        act.wait_ge(gram_done, t * UNITS + n + 1)
                        for q in (2, 3):
                            ins = nc.scalar.copy(
                                gram[QP * q:QP * q + QP, t % 2, :, UNIT * n:UNIT * n + UNIT].rearrange("g f u -> g u f"),
                                gps[QP * q:QP * q + QP, n % 2, :, NF * q:NF * q + NF])
                        ins.then_inc(cut_act, 1)
                    act.wait_ge(pairs_ready, 2 * (t + 1))
                    if t:
                        act.wait_ge(pairs_done, t)
                    start = pairs[:, 0, 0:1]
                    picked = bass.AP(start.tensor, start.offset, [list(start.ap[0]), [QP + 1, NF], [QP, DELTAS]])
                    nc.scalar.copy(z[:].rearrange("p (g e) -> p g e", g=NF), picked).then_inc(z_ready, 1)
                elif step == "pairs":
                    if t >= 2:
                        act.wait_ge(l1_done, 2 * (t - 1))
                    act.wait_ge(pairs_done, t + 1)
                    b = bank(step, t)
                    nc.scalar.copy(zt[:, t % 2, :, :], ring[0:ZK, b, 0:ZC * LANES].rearrange("k (c p) -> k c p", c=ZC)
                                   ).then_inc(zt_ready, 1)
                elif step == "l1":
                    if t == 0:
                        act.wait_ge(w_in, 16 * 6)
                    if t >= 2:
                        act.wait_ge(l2_done, M2 * (t - 1))
                    b = bank(step, t, 0)
                    act.wait_ge(l1_done, 2 * t + 1)
                    for m in range(M1 // 2):
                        nc.scalar.activation(h1[:, t % 2, m, :], ring[:, b, m * LANES:(m + 1) * LANES], ACT.Relu,
                                             bias=b1_sb[:, m:m + 1]).then_inc(h1_act, 1)
                elif step == "l2":
                    if t >= 2:
                        act.wait_ge(l3_done, t - 1)
                    b = bank(step, t)
                    act.wait_ge(l2_done, M2 * t + 1)
                    nc.scalar.activation(h2[:, t % 2, 0, :], ring[:, b, 0:LANES], ACT.Relu,
                                         bias=b2_sb[:, 0:1]).then_inc(h2_act, 1)
                elif step == "l3":
                    b = bank(step, t)
                    act.wait_ge(l3_done, t + 1)
                    nc.scalar.copy(y[0:1, :].rearrange("o (u q t) -> o q u t", q=Q, t=TILES)[:, :, :, t],
                                   ring[0:1, b, 0:LANES].rearrange("o (q u) -> o q u", q=Q)
                                   ).then_inc(y_ready, 1)

        @block.vector
        def _(dve):
            nc.vector.memset(ident[:], 1.0).then_inc(pad_set, 1)
            nc.vector.memset(emb[:, :, :, NF:QP], 0.0).then_inc(pad_set, 1)
            dve.wait_ge(row_set, 1)
            nc.vector.tensor_copy(row_f[:], row_i[:]).then_inc(row_ready, 1)
            dve.wait_ge(row_ready, 1)

            for step, t in ORDER:
                if step == "look":
                    dve.wait_ge(idb_in[t], 16)
                    for half in range(2):
                        n = 2 * t + half
                        if n >= OH_RING:
                            dve.wait_ge(oh_used, n - OH_RING + 1)
                        for k in range(HALF):
                            chunk = HALF * half + k
                            ins = nc.vector.tensor_scalar(onehot[:, n % OH_RING, k, :], ids_b[:, t, :],
                                                          row_f[:, chunk:chunk + 1], None, ALU.is_equal)
                        ins.then_inc(oh_ready, 1)
                        if half == 0:
                            dve.wait_ge(hi_ready, t + 1)
                            if t >= HL_RING:
                                dve.wait_ge(oh_used, 2 * (t - HL_RING + 1))
                            nc.vector.tensor_tensor(lo[:, t % HL_RING, :], raw[:, t % RAW_RING, :],
                                                    hi[:, t % HL_RING, :].bitcast(F32),
                                                    ALU.subtract).then_inc(lo_ready, 1)
                elif step == "turn":
                    for g, slots in enumerate(GROUPS):
                        if by_act(g):
                            continue
                        dve.wait_ge(turned, t * len(GROUPS) + g + 1)
                        b = bank(step, t, g)
                        n = len(slots)
                        nc.vector.tensor_copy(emb_slots(t, slots[0], n),
                                              ring[:, b, 0:n * LANES].rearrange("d (f p) -> d f p", f=n)
                                              ).then_inc(emb_dve, 1)
                elif step == "gram":
                    if t >= 2:
                        dve.wait_ge(pairs_ready, 2 * (t - 1))
                    for n in range(UNITS):
                        dve.wait_ge(gram_done, t * UNITS + n + 1)
                        for q in (0, 1):
                            ins = nc.vector.tensor_copy(
                                gram[QP * q:QP * q + QP, t % 2, :, UNIT * n:UNIT * n + UNIT].rearrange("g f u -> g u f"),
                                gps[QP * q:QP * q + QP, n % 2, :, NF * q:NF * q + NF])
                        ins.then_inc(cut_dve, 1)
                    dve.wait_ge(cut_dve, UNITS * (t + 1))
                    dve.wait_ge(cut_act, UNITS * (t + 1))
                    if t:
                        dve.wait_ge(z_ready, t)
                    nc.vector.transpose(pairs[:, 0:NF - 1, :], gram[:, t % 2, 1:NF, :]).then_inc(pairs_ready, 1)
                    nc.vector.transpose(pairs[:, NF - 1:, :], gram[:, t % 2, 0:DELTAS, :]).then_inc(pairs_ready, 1)
                elif step == "l1":
                    if t == 0:
                        dve.wait_ge(w_in, 16 * 6)
                    if t >= 2:
                        dve.wait_ge(l2_done, M2 * (t - 1))
                    b = bank(step, t, 1)
                    dve.wait_ge(l1_done, 2 * t + 2)
                    for n in range(M1 // 2):
                        m = M1 // 2 + n
                        nc.vector.tensor_scalar(h1[:, t % 2, m, :], ring[:, b, n * LANES:(n + 1) * LANES],
                                                b1_sb[:, m:m + 1], 0.0, ALU.add, ALU.max).then_inc(h1_dve, 1)
                elif step == "l2":
                    if t >= 2:
                        dve.wait_ge(l3_done, t - 1)
                    b = bank(step, t, 1)
                    dve.wait_ge(l2_done, M2 * t + 2)
                    nc.vector.tensor_scalar(h2[:, t % 2, 1, :], ring[:, b, 0:LANES],
                                            b2_sb[:, 1:2], 0.0, ALU.add, ALU.max).then_inc(h2_dve, 1)

        @block.tensor
        def _(pe):
            def wait_emptied(step, t, part=0):
                n = USES.index((step, t, part))
                if n < BANKS:
                    return
                was, i, g = USES[n - BANKS]
                if was == "look":
                    pe.wait_ge(emb_look, i + 1)
                elif was == "turn" and by_act(g):
                    pe.wait_ge(emb_act, i * ACT_GROUPS + sum(by_act(x) for x in range(g + 1)))
                elif was == "turn":
                    pe.wait_ge(emb_dve, i * DVE_GROUPS + sum(not by_act(x) for x in range(g + 1)))
                elif was == "pairs":
                    pe.wait_ge(zt_ready, i + 1)
                elif was == "l1":
                    pe.wait_ge(h1_dve if g else h1_act, M1 // 2 * (i + 1))
                elif was == "l2":
                    pe.wait_ge(h2_dve if g else h2_act, i + 1)
                elif was == "l3":
                    pe.wait_ge(y_ready, i + 1)

            for step, t in ORDER:
                b = bank(step, t) if step in TAKES else None
                if step == "look":
                    wait_emptied(step, t)
                    pe.wait_ge(hi_ready, t + 1)
                    for half in range(2):
                        n = 2 * t + half
                        pe.wait_ge(oh_ready, n + 1)
                        if half == 0:
                            pe.wait_ge(lo_ready, t + 1)
                        for k in range(HALF):
                            chunk = HALF * half + k
                            for part in (hi, lo):
                                mm = nc.tensor.matmul(ring[:, b, :], part[:, t % HL_RING, chunk * D:(chunk + 1) * D],
                                                      onehot[:, n % OH_RING, k, :],
                                                      start=(chunk == 0 and part is hi),
                                                      stop=(chunk == KC - 1 and part is lo))
                        mm.then_inc(oh_used, 1)
                elif step == "turn":
                    if t == 0:
                        pe.wait_ge(ident_set, 1)
                        pe.wait_ge(bot_in, 16)
                    for g, slots in enumerate(GROUPS):
                        wait_emptied(step, t, g)
                        gathered = sum(s > 0 for s in slots)
                        pe.wait_ge(rows_in[t][g], 16 * gathered)
                        bg = bank(step, t, g)
                        for n, slot in enumerate(slots):
                            src = rows[:, t, slot - 1, :] if slot else bot[:, t, :]
                            mm = nc.tensor.transpose(ring[:, bg, n * LANES:(n + 1) * LANES], src, ident[:])
                        mm.then_inc(turned, 1)
                elif step == "gram":
                    if t == 0:
                        pe.wait_ge(emb_look, NL)
                        pe.wait_ge(pad_set, 2)
                    pe.wait_ge(emb_act, ACT_GROUPS * (t + 1))
                    pe.wait_ge(emb_dve, DVE_GROUPS * (t + 1))
                    for n in range(UNITS):
                        unit = t * UNITS + n
                        if unit >= 2:
                            pe.wait_ge(cut_act, unit - 1)
                            pe.wait_ge(cut_dve, unit - 1)
                        for k in range(UNIT):
                            four = emb[:, t, Q * (UNIT * n + k):Q * (UNIT * n + k + 1), :]
                            mm = nc.tensor.matmul(gps[:, n % 2, k, 0:Q * NF], four.rearrange("d q f -> d (q f)"),
                                                  four[:, :, 0:NF], start=True, stop=True)
                        mm.then_inc(gram_done, 1)
                elif step == "pairs":
                    wait_emptied(step, t)
                    pe.wait_ge(z_ready, t + 1)
                    for c in range(ZC):
                        mm = nc.tensor.transpose(ring[0:ZK, b, c * LANES:(c + 1) * LANES],
                                                 z[:, c * ZK:(c + 1) * ZK], ident[:])
                    mm.then_inc(pairs_done, 1)
                elif step == "l1":
                    if t == 0:
                        pe.wait_ge(w_in, 16 * 6)
                    pe.wait_ge(zt_ready, t + 1)
                    for m in range(M1):
                        half, n = divmod(m, M1 // 2)
                        if n == 0:
                            wait_emptied(step, t, half)
                        o = ring[:, bank(step, t, half), n * LANES:(n + 1) * LANES]
                        nc.tensor.matmul(o, w1b[:, m * 128:(m + 1) * 128], emb[:, t, :, 0].rearrange("d (u q) -> d q u", q=Q),
                                         start=True, stop=False)
                        for c in range(ZC):
                            mm = nc.tensor.matmul(o, w1z[:, c, m * 128:(m + 1) * 128], zt[:, t % 2, c, :],
                                                  start=False, stop=(c == ZC - 1))
                        if n:
                            mm.then_inc(l1_done, 1)
                elif step == "l2":
                    for m in range(M2):
                        wait_emptied(step, t, m)
                        o = ring[:, bank(step, t, m), 0:LANES]
                        for k in range(M1):
                            half, n = divmod(k, M1 // 2)
                            if m == 0:
                                pe.wait_ge(h1_dve if half else h1_act, M1 // 2 * t + n + 1)
                            mm = nc.tensor.matmul(o, w2_sb[:, k, m * 128:(m + 1) * 128], h1[:, t % 2, k, :],
                                                  start=(k == 0), stop=(k == M1 - 1))
                        mm.then_inc(l2_done, 1)
                elif step == "l3":
                    wait_emptied(step, t)
                    for k in range(M2):
                        pe.wait_ge(h2_dve if k % 2 else h2_act, t + 1)
                        mm = nc.tensor.matmul(ring[0:1, b, 0:LANES], w3_sb[:, k:k + 1], h2[:, t % 2, k, :],
                                              start=(k == 0), stop=(k == M2 - 1))
                    mm.then_inc(l3_done, 1)


def pair_rows():
    rows = []
    for g in range(NF):
        for delta in range(1, DELTAS + 1):
            i, j = sorted((SLOTS[g], SLOTS[(g + delta) % NF]))
            rows.append(i * (2 * NF - i - 1) // 2 + j - i - 1)
    return rows


def kernel(**inputs):
    import numpy as np
    import concourse.bacc as bacc
    from concourse.bass_utils import run_bass_kernel_spmd

    nc = bacc.Bacc("TRN2", target_bir_lowering=False, num_devices=1)
    arrays = {}

    def given(name, array):
        array = np.ascontiguousarray(array)
        arrays[name] = array
        return nc.dram_tensor(name, array.shape, mybir.dt.from_np(array.dtype), kind="ExternalInput").ap()

    w1 = np.asarray(inputs["W_top1"])
    order = pair_rows() + list(range(NF * DELTAS, w1.shape[0]))
    ids = np.asarray(inputs["ids"])
    bottom_d = given("bottom", inputs["r_bottom_output"])
    ids_d = given("ids", ids)
    ids_t_d = given("ids_t", ids.T)
    tables_d = [given(f"tbl_{i}", inputs[f"tbl_{i}"]) for i in range(TABLES)]
    w1_d = given("w1", w1[order])
    b1_d = given("b1", np.asarray(inputs["b_top1"]).reshape(M1, 128).T)
    w2_d = given("w2", inputs["W_top2"])
    b2_d = given("b2", np.asarray(inputs["b_top2"]).reshape(M2, 128).T)
    w3_d = given("w3", np.asarray(inputs["W_top3"]).reshape(M2, 128).T)
    out_d = nc.dram_tensor("out", (B, 1), F32, kind="ExternalOutput").ap()
    tower(nc, bottom_d, ids_d, ids_t_d, tables_d, w1_d, b1_d, w2_d, b2_d, w3_d, out_d)
    return run_bass_kernel_spmd(nc, [arrays], core_ids=[0]).results[0]["out"]
```

```python
from contextlib import ExitStack

import concourse.bass as bass
from concourse import mybir

F32 = mybir.dt.float32
F32R = mybir.dt.float32r
I32 = mybir.dt.int32
ALU = mybir.AluOpType
ACT = mybir.ActivationFunctionType

B = 512
D = 128
TABLES = 26
NF = TABLES + 1
LANES = 128
TILES = B // LANES
Q = 4
QP = 32
U = LANES // Q
LOOKED_UP = [1, 2, 4, 16, 17, 18, 20, 21, 24]
GATHERED = [i for i in range(TABLES) if i not in LOOKED_UP]
SLOTS = [0] + [i + 1 for i in GATHERED] + [i + 1 for i in LOOKED_UP]
NG = len(GATHERED)
NL = len(LOOKED_UP)
TURNED = NG + 1
GROUP = 4
GROUPS = [range(a, min(a + GROUP, TURNED)) for a in range(0, TURNED, GROUP)]
ROWS = 1000
KP = 125
KC = ROWS // KP
HALF = KC // 2
DELTAS = NF // 2
ZG = 9
ZC = NF // ZG
ZK = ZG * DELTAS
H1, H2 = 512, 256
M1, M2 = H1 // 128, H2 // 128
GM = (Q - 1) * QP + NF
UNIT = 8
UNITS = U // UNIT
BANKS = 4
WARM_UP = 14
OH_RING, HL_RING, RAW_RING = 3, 2, 3

def work_order():
    turns = [("turn", t, g) for t in range(TILES) for g in range(len(GROUPS))]
    order = []
    for j in range(NL):
        order.append(("look", j, 0))
        if j:
            order.append(turns.pop(0))
    order.append(turns.pop(0))
    def turn(t, leave):
        while turns and turns[0][1] <= t and sum(x[1] <= t for x in turns) > leave:
            order.append(turns.pop(0))

    for t in range(TILES):
        turn(t, 2)
        if t >= 2:
            order.append(("l2", t - 2, 0))
        turn(t, 1)
        if t >= 2:
            order.append(("l3", t - 2, 0))
        turn(t, 0)
        if t >= 2:
            order.append(("pairs", t - 1, 0))
        order.append(("gram", t, 0))
        if t == 0:
            turn(1, 0)
        if t == 1:
            order.append(("pairs", t - 1, 0))
        order.append(("gram", t, 1))
        if t >= 1:
            order.append(("l1", t - 1, 0))
    t = TILES - 1
    return order + [("pairs", t, 0), ("l2", t - 1, 0), ("l1", t, 0), ("l3", t - 1, 0), ("l2", t, 0), ("l3", t, 0)]


ORDER = work_order()

BANKS_OF = {"look": [0], "pairs": [0], "l1": [0, 1], "l2": [0, 1], "l3": [0], "gram": []}
USES = [(step, i, p) for step, i, part in ORDER for p in BANKS_OF.get(step, [part])]


def bank(step, i, part=0):
    return USES.index((step, i, part)) % BANKS


def tower(nc, bottom, ids, ids_t, tables, w1, b1, w2, b2, w3, out):
    ctx = ExitStack()
    with ctx:
        def sb(name, shape, dt=F32):
            return ctx.enter_context(nc.sbuf_tensor(name, shape, dt))

        def sem(name):
            return ctx.enter_context(nc.semaphore(name))

        ids_sb = sb("ids_sb", [128, TILES * TABLES], I32)
        bot = sb("bot", [128, TILES, D])
        rows = sb("rows", [128, TILES, NG, D])
        emb = sb("emb", [128, TILES, LANES, QP])
        gram = sb("gram", [128, 2, NF, U])
        pairs = sb("pairs", [128, NF - 1 + DELTAS, QP])
        z = sb("z", [128, NF * DELTAS])
        zt = sb("zt", [ZK, 2, ZC, LANES])
        h1 = sb("h1", [128, 2, M1, LANES])
        h2 = sb("h2", [128, 2, M2, LANES])
        y = sb("y", [1, B])
        raw = sb("raw", [KP, RAW_RING, KC * D])
        hi = sb("hi", [KP, HL_RING, KC * D], F32R)
        lo = sb("lo", [KP, HL_RING, KC * D], F32R)
        ids_b = sb("ids_b", [KP, HL_RING, B], I32)
        ids_f = sb("ids_f", [KP, HL_RING, B])
        onehot = sb("onehot", [KP, OH_RING, HALF, B], F32R)
        first_i = sb("first_i", [KP, 1], I32)
        first_f = sb("first_f", [KP, 1])
        ident = sb("ident", [128, 128])
        w1z = sb("w1z", [ZK, ZC, H1])
        w1b = sb("w1b", [128, H1])
        w2_sb = sb("w2_sb", [128, M1, H2])
        w3_sb = sb("w3_sb", [128, M2])
        b1_sb = sb("b1_sb", [128, M1])
        b2_sb = sb("b2_sb", [128, M2])

        ring = ctx.enter_context(nc.psum_tensor("ring", [128, BANKS, 512], F32))
        gps = ctx.enter_context(nc.psum_tensor("gps", [128, 2, UNIT, 128], F32))

        ids_in = sem("ids_in")
        bot_in = sem("bot_in")
        w_in = sem("w_in")
        raw_in = [sem(f"raw_in{k}") for k in range(RAW_RING)]
        idb_in = [sem(f"idb_in{j}") for j in range(NL)]
        rows_in = [[sem(f"rows_in{t}_{g}") for g in range(len(GROUPS))] for t in range(TILES)]
        out_done = sem("out_done")
        ident_set = sem("ident_set")
        blank_set = sem("blank_set")
        ones_set = sem("ones_set")
        pad_set = sem("pad_set")
        row_set = sem("row_set")
        row_ready = sem("row_ready")
        idf_ready = sem("idf_ready")
        hi_ready = sem("hi_ready")
        lo_ready = sem("lo_ready")
        oh_ready = sem("oh_ready")
        oh_used = sem("oh_used")
        turned = sem("turned")
        emb_look = sem("emb_look")
        emb_turned = sem("emb_turned")
        gram_done = sem("gram_done")
        cut_act = sem("cut_act")
        cut_dve = sem("cut_dve")
        pairs_ready = sem("pairs_ready")
        z_ready = sem("z_ready")
        pairs_done = sem("pairs_done")
        zt_ready = sem("zt_ready")
        l1_done = sem("l1_done")
        h1_act = sem("h1_act")
        h1_dve = sem("h1_dve")
        l2_done = sem("l2_done")
        h2_act = sem("h2_act")
        h2_dve = sem("h2_dve")
        l3_done = sem("l3_done")
        y_ready = sem("y_ready")

        def emb_slots(t, first, count):
            return emb[:, t, :, first:first + count].rearrange("d p f -> d f p")

        block = ctx.enter_context(nc.Block())

        @block.sync
        def _(sp):
            sp.dma_start(ids_sb[:], ids.rearrange("(p t) f -> p (t f)", t=TILES)).then_inc(ids_in, 16)

            def load_ids(j):
                if j >= HL_RING:
                    sp.wait_ge(idf_ready, j - HL_RING + 1)
                row = ids_t[LOOKED_UP[j]:LOOKED_UP[j] + 1, :]
                sp.dma_start(ids_b[:, j % HL_RING, :], row.broadcast_to([KP, B])).then_inc(idb_in[j], 16)

            for j in range(NL):
                load_ids(j)
                if j >= RAW_RING:
                    sp.wait_ge(lo_ready, j - RAW_RING + 1)
                sp.dma_start(raw[:, j % RAW_RING, :], tables[LOOKED_UP[j]].rearrange("(p k) d -> p (k d)", k=KC)
                             ).then_inc(raw_in[j % RAW_RING], 16)
                if j == RAW_RING - 1:
                    sp.dma_start(bot[:], bottom.rearrange("(p t) d -> p t d", t=TILES)).then_inc(bot_in, 16)
                    sp.dma_start(w1z[:], w1[0:ZC * ZK, :].rearrange("(c k) n -> k c n", c=ZC)).then_inc(w_in, 16)
                    sp.dma_start(w1b[:], w1[ZC * ZK:, :]).then_inc(w_in, 16)
                    sp.dma_start(w2_sb[:], w2.rearrange("(c k) n -> k c n", c=M1)).then_inc(w_in, 16)
                    sp.dma_start(w3_sb[:], w3).then_inc(w_in, 16)
                    sp.dma_start(b1_sb[:], b1).then_inc(w_in, 16)
                    sp.dma_start(b2_sb[:], b2).then_inc(w_in, 16)
            sp.wait_ge(y_ready, TILES)
            sp.dma_start(out.rearrange("b o -> o b"), y[:]).then_inc(out_done, 16)
            sp.wait_ge(out_done, 16)

        @block.gpsimd
        def _(pool):
            nc.gpsimd.iota(first_i[:], pattern=[[1, 1]], base=0, channel_multiplier=-KC).then_inc(row_set, 1)
            pool.wait_ge(row_set, 1)
            pool.wait_ge(ones_set, 1)
            nc.gpsimd.affine_select(out=ident[:], in_=ident[:], compare_op=ALU.is_equal, fill=0.0, base=0,
                                    pattern=[[-1, 128]], channel_multiplier=1).then_inc(ident_set, 1)
            pool.wait_ge(ident_set, 1)
            nc.gpsimd.memset(gram[QP * (Q - 1):, :, :, :], 0.0).then_inc(blank_set, 1)
            pool.wait_ge(ids_in, 16)

            def gather(t, g):
                for slot in GROUPS[g]:
                    if slot == 0:
                        continue
                    table = GATHERED[slot - 1]
                    col = t * TABLES + table
                    nc.gpsimd.indirect_dma_start(
                        out=rows[:, t, slot - 1, :], out_offset=None, in_=tables[table],
                        in_offset=bass.IndirectOffsetOnAxis(ap=ids_sb[:, col:col + 1], axis=0),
                    ).then_inc(rows_in[t][g], 16)

            for t in range(TILES):
                for g in range(len(GROUPS)):
                    gather(t, g)

        @block.scalar
        def _(act):

            def float_ids(j):
                act.wait_ge(idb_in[j], 16)
                if j >= HL_RING:
                    act.wait_ge(oh_ready, 2 * (j - HL_RING + 1))
                if j == 0:
                    act.wait_ge(row_ready, 1)
                nc.scalar.activation(ids_f[:, j % HL_RING, :], ids_b[:, j % HL_RING, :], ACT.Identity,
                                     bias=first_f[:]).then_inc(idf_ready, 1)

            def split(j):
                act.wait_ge(raw_in[j % RAW_RING], 16 * (j // RAW_RING + 1))
                if j >= HL_RING:
                    act.wait_ge(oh_used, 2 * (j - HL_RING + 1))
                nc.scalar.copy(hi[:, j % HL_RING, :], raw[:, j % RAW_RING, :]).then_inc(hi_ready, 1)

            for step, t, part in ORDER:
                if step == "look":
                    if t == 0:
                        for j in range(HL_RING):
                            float_ids(j)
                            split(j)
                    elif t + 1 < NL:
                        float_ids(t + 1)
                        split(t + 1)
                    act.wait_ge(oh_used, 2 * (t + 1))
                    b = bank(step, t)
                    slot = TURNED + t
                    nc.scalar.copy(emb[:, :, :, slot], ring[:, b, :].rearrange("d (p t) -> d t p", t=TILES)
                                   ).then_inc(emb_look, 1)
                elif step == "turn":
                    act.wait_ge(turned, t * len(GROUPS) + part + 1)
                    b = bank(step, t, part)
                    slots = GROUPS[part]
                    n = len(slots)
                    nc.scalar.copy(emb_slots(t, slots[0], n),
                                   ring[:, b, 0:n * LANES].rearrange("d (f p) -> d f p", f=n)
                                   ).then_inc(emb_turned, 1)
                elif step == "gram":
                    if t == 0:
                        act.wait_ge(blank_set, 1)
                    if t >= 2:
                        act.wait_ge(pairs_ready, 2 * (t - 1))
                    for n in range(part * UNITS // 2, (part + 1) * UNITS // 2):
                        act.wait_ge(gram_done, t * UNITS + n + 1)
                        for q in (2, 3):
                            ins = nc.scalar.copy(
                                gram[QP * q:min(QP * q + QP, GM), t % 2, :, UNIT * n:UNIT * n + UNIT].rearrange("g f u -> g u f"),
                                gps[QP * q:min(QP * q + QP, GM), n % 2, :, NF * q:NF * q + NF])
                        ins.then_inc(cut_act, 1)
                elif step == "pairs":
                    if t >= 2:
                        act.wait_ge(l1_done, 2 * (t - 1))
                    act.wait_ge(pairs_done, t + 1)
                    b = bank(step, t)
                    nc.scalar.copy(zt[:, t % 2, :, :], ring[0:ZK, b, 0:ZC * LANES].rearrange("k (c p) -> k c p", c=ZC)
                                   ).then_inc(zt_ready, 1)
                elif step == "l1":
                    if t == 0:
                        act.wait_ge(w_in, 16 * 6)
                    if t >= 2:
                        act.wait_ge(l2_done, M2 * (t - 1))
                    b = bank(step, t, 0)
                    act.wait_ge(l1_done, 2 * t + 1)
                    for m in range(M1 // 2):
                        nc.scalar.activation(h1[:, t % 2, m, :], ring[:, b, m * LANES:(m + 1) * LANES], ACT.Relu,
                                             bias=b1_sb[:, m:m + 1]).then_inc(h1_act, 1)
                elif step == "l2":
                    if t >= 2:
                        act.wait_ge(l3_done, t - 1)
                    b = bank(step, t)
                    act.wait_ge(l2_done, M2 * t + 1)
                    nc.scalar.activation(h2[:, t % 2, 0, :], ring[:, b, 0:LANES], ACT.Relu,
                                         bias=b2_sb[:, 0:1]).then_inc(h2_act, 1)
                elif step == "l3":
                    b = bank(step, t)
                    act.wait_ge(l3_done, t + 1)
                    nc.scalar.copy(y[0:1, :].rearrange("o (u q t) -> o q u t", q=Q, t=TILES)[:, :, :, t],
                                   ring[0:1, b, 0:LANES].rearrange("o (q u) -> o q u", q=Q)
                                   ).then_inc(y_ready, 1)

        @block.vector
        def _(dve):
            nc.vector.memset(ident[:], 1.0).then_inc(ones_set, 1)
            dve.wait_ge(row_set, 1)
            nc.vector.tensor_copy(first_f[:], first_i[:]).then_inc(row_ready, 1)
            nc.vector.memset(emb[:, :, :, NF:QP], 0.0).then_inc(pad_set, 1)

            for step, t, part in ORDER:
                if step == "look":
                    dve.wait_ge(idf_ready, t + 1)
                    for half in range(2):
                        n = 2 * t + half
                        if n >= OH_RING:
                            dve.wait_ge(oh_used, n - OH_RING + 1)
                        for k in range(HALF):
                            chunk = HALF * half + k
                            ins = nc.vector.tensor_scalar(onehot[:, n % OH_RING, k, :], ids_f[:, t % HL_RING, :],
                                                          float(chunk), None, ALU.is_equal)
                        ins.then_inc(oh_ready, 1)
                        if half == 0:
                            dve.wait_ge(hi_ready, t + 1)
                            if t >= HL_RING:
                                dve.wait_ge(oh_used, 2 * (t - HL_RING + 1))
                            nc.vector.tensor_tensor(lo[:, t % HL_RING, :], raw[:, t % RAW_RING, :],
                                                    hi[:, t % HL_RING, :].bitcast(F32),
                                                    ALU.subtract).then_inc(lo_ready, 1)
                elif step == "gram":
                    if t >= 2:
                        dve.wait_ge(pairs_ready, 2 * (t - 1))
                    for n in range(part * UNITS // 2, (part + 1) * UNITS // 2):
                        dve.wait_ge(gram_done, t * UNITS + n + 1)
                        for q in (0, 1):
                            ins = nc.vector.tensor_copy(
                                gram[QP * q:QP * q + QP, t % 2, :, UNIT * n:UNIT * n + UNIT].rearrange("g f u -> g u f"),
                                gps[QP * q:QP * q + QP, n % 2, :, NF * q:NF * q + NF])
                        ins.then_inc(cut_dve, 1)
                    if part == 0:
                        continue
                    dve.wait_ge(cut_dve, UNITS * (t + 1))
                    dve.wait_ge(cut_act, UNITS * (t + 1))
                    if t:
                        dve.wait_ge(z_ready, t)
                    nc.vector.transpose(pairs[:, 0:NF - 1, :], gram[:, t % 2, 1:NF, :]).then_inc(pairs_ready, 1)
                    nc.vector.transpose(pairs[:, NF - 1:, :], gram[:, t % 2, 0:DELTAS, :]).then_inc(pairs_ready, 1)
                    dve.wait_ge(pairs_ready, 2 * (t + 1))
                    if t:
                        dve.wait_ge(pairs_done, t)
                    start = pairs[:, 0, 0:1]
                    picked = bass.AP(start.tensor, start.offset, [list(start.ap[0]), [QP + 1, NF], [QP, DELTAS]])
                    nc.vector.tensor_copy(z[:].rearrange("p (g e) -> p g e", g=NF), picked).then_inc(z_ready, 1)
                elif step == "l1":
                    if t == 0:
                        dve.wait_ge(w_in, 16 * 6)
                    if t >= 2:
                        dve.wait_ge(l2_done, M2 * (t - 1))
                    b = bank(step, t, 1)
                    dve.wait_ge(l1_done, 2 * t + 2)
                    for n in range(M1 // 2):
                        m = M1 // 2 + n
                        nc.vector.tensor_scalar(h1[:, t % 2, m, :], ring[:, b, n * LANES:(n + 1) * LANES],
                                                b1_sb[:, m:m + 1], 0.0, ALU.add, ALU.max).then_inc(h1_dve, 1)
                elif step == "l2":
                    if t >= 2:
                        dve.wait_ge(l3_done, t - 1)
                    b = bank(step, t, 1)
                    dve.wait_ge(l2_done, M2 * t + 2)
                    nc.vector.tensor_scalar(h2[:, t % 2, 1, :], ring[:, b, 0:LANES],
                                            b2_sb[:, 1:2], 0.0, ALU.add, ALU.max).then_inc(h2_dve, 1)

        @block.tensor
        def _(pe):
            def wait_emptied(step, t, part=0):
                n = USES.index((step, t, part))
                if n < BANKS:
                    return
                was, i, g = USES[n - BANKS]
                if was == "look":
                    pe.wait_ge(emb_look, i + 1)
                elif was == "turn":
                    pe.wait_ge(emb_turned, i * len(GROUPS) + g + 1)
                elif was == "pairs":
                    pe.wait_ge(zt_ready, i + 1)
                elif was == "l1":
                    pe.wait_ge(h1_dve if g else h1_act, M1 // 2 * (i + 1))
                elif was == "l2":
                    pe.wait_ge(h2_dve if g else h2_act, i + 1)
                elif was == "l3":
                    pe.wait_ge(y_ready, i + 1)

            pe.wait_ge(ident_set, 1)
            for n in range(WARM_UP):
                nc.tensor.matmul(gps[:, 0, 0, :], ident[:], ident[:], start=True, stop=True)

            for step, t, part in ORDER:
                b = bank(step, t, part) if step != "gram" else None
                if step == "look":
                    wait_emptied(step, t)
                    pe.wait_ge(hi_ready, t + 1)
                    for half in range(2):
                        n = 2 * t + half
                        pe.wait_ge(oh_ready, n + 1)
                        for part_of in (hi, lo):
                            if part_of is lo and half == 0:
                                pe.wait_ge(lo_ready, t + 1)
                            for k in range(HALF):
                                chunk = HALF * half + k
                                mm = nc.tensor.matmul(ring[:, b, :],
                                                      part_of[:, t % HL_RING, chunk * D:(chunk + 1) * D],
                                                      onehot[:, n % OH_RING, k, :],
                                                      start=(chunk == 0 and part_of is hi),
                                                      stop=(chunk == KC - 1 and part_of is lo))
                        mm.then_inc(oh_used, 1)
                elif step == "turn":
                    if (t, part) == (0, 0):
                        pe.wait_ge(bot_in, 16)
                    slots = GROUPS[part]
                    wait_emptied(step, t, part)
                    pe.wait_ge(rows_in[t][part], 16 * sum(s > 0 for s in slots))
                    for n, slot in enumerate(slots):
                        src = rows[:, t, slot - 1, :] if slot else bot[:, t, :]
                        mm = nc.tensor.transpose(ring[:, b, n * LANES:(n + 1) * LANES], src, ident[:])
                    mm.then_inc(turned, 1)
                elif step == "gram":
                    if t == 0:
                        pe.wait_ge(emb_look, NL)
                        pe.wait_ge(pad_set, 1)
                    pe.wait_ge(emb_turned, (t + 1) * len(GROUPS))
                    for n in range(part * UNITS // 2, (part + 1) * UNITS // 2):
                        unit = t * UNITS + n
                        if unit >= 2:
                            pe.wait_ge(cut_act, unit - 1)
                            pe.wait_ge(cut_dve, unit - 1)
                        for k in range(UNIT):
                            four = emb[:, t, Q * (UNIT * n + k):Q * (UNIT * n + k + 1), :]
                            mm = nc.tensor.matmul(gps[0:GM, n % 2, k, 0:Q * NF], four.rearrange("d q f -> d (q f)")[:, 0:GM],
                                                  four[:, :, 0:NF], start=True, stop=True)
                        mm.then_inc(gram_done, 1)
                elif step == "pairs":
                    wait_emptied(step, t)
                    pe.wait_ge(z_ready, t + 1)
                    for c in range(ZC):
                        mm = nc.tensor.transpose(ring[0:ZK, b, c * LANES:(c + 1) * LANES],
                                                 z[:, c * ZK:(c + 1) * ZK], ident[:])
                    mm.then_inc(pairs_done, 1)
                elif step == "l1":
                    if t == 0:
                        pe.wait_ge(w_in, 16 * 6)
                    pe.wait_ge(zt_ready, t + 1)
                    for m in range(M1):
                        half, n = divmod(m, M1 // 2)
                        if n == 0:
                            wait_emptied(step, t, half)
                        o = ring[:, bank(step, t, half), n * LANES:(n + 1) * LANES]
                        nc.tensor.matmul(o, w1b[:, m * 128:(m + 1) * 128], emb[:, t, :, 0].rearrange("d (u q) -> d q u", q=Q),
                                         start=True, stop=False)
                        for c in range(ZC):
                            mm = nc.tensor.matmul(o, w1z[:, c, m * 128:(m + 1) * 128], zt[:, t % 2, c, :],
                                                  start=False, stop=(c == ZC - 1))
                        if n:
                            mm.then_inc(l1_done, 1)
                elif step == "l2":
                    for m in range(M2):
                        wait_emptied(step, t, m)
                        o = ring[:, bank(step, t, m), 0:LANES]
                        for k in range(M1):
                            half, n = divmod(k, M1 // 2)
                            if m == 0:
                                pe.wait_ge(h1_dve if half else h1_act, M1 // 2 * t + n + 1)
                            mm = nc.tensor.matmul(o, w2_sb[:, k, m * 128:(m + 1) * 128], h1[:, t % 2, k, :],
                                                  start=(k == 0), stop=(k == M1 - 1))
                        mm.then_inc(l2_done, 1)
                elif step == "l3":
                    wait_emptied(step, t)
                    for k in range(M2):
                        pe.wait_ge(h2_dve if k % 2 else h2_act, t + 1)
                        mm = nc.tensor.matmul(ring[0:1, b, 0:LANES], w3_sb[:, k:k + 1], h2[:, t % 2, k, :],
                                              start=(k == 0), stop=(k == M2 - 1))
                    mm.then_inc(l3_done, 1)


def pair_rows():
    rows = []
    for g in range(NF):
        for delta in range(1, DELTAS + 1):
            i, j = sorted((SLOTS[g], SLOTS[(g + delta) % NF]))
            rows.append(i * (2 * NF - i - 1) // 2 + j - i - 1)
    return rows


def kernel(**inputs):
    import numpy as np
    import concourse.bacc as bacc
    from concourse.bass_utils import run_bass_kernel_spmd

    nc = bacc.Bacc("TRN2", target_bir_lowering=False, num_devices=1)
    arrays = {}

    def given(name, array):
        array = np.ascontiguousarray(array)
        arrays[name] = array
        return nc.dram_tensor(name, array.shape, mybir.dt.from_np(array.dtype), kind="ExternalInput").ap()

    w1 = np.asarray(inputs["W_top1"])
    order = pair_rows() + list(range(NF * DELTAS, w1.shape[0]))
    ids = np.asarray(inputs["ids"])
    bottom_d = given("bottom", inputs["r_bottom_output"])
    ids_d = given("ids", ids)
    ids_t_d = given("ids_t", ids.T)
    tables_d = [given(f"tbl_{i}", inputs[f"tbl_{i}"]) for i in range(TABLES)]
    w1_d = given("w1", w1[order])
    b1_d = given("b1", np.asarray(inputs["b_top1"]).reshape(M1, 128).T)
    w2_d = given("w2", inputs["W_top2"])
    b2_d = given("b2", np.asarray(inputs["b_top2"]).reshape(M2, 128).T)
    w3_d = given("w3", np.asarray(inputs["W_top3"]).reshape(M2, 128).T)
    out_d = nc.dram_tensor("out", (B, 1), F32, kind="ExternalOutput").ap()
    tower(nc, bottom_d, ids_d, ids_t_d, tables_d, w1_d, b1_d, w2_d, b2_d, w3_d, out_d)
    return run_bass_kernel_spmd(nc, [arrays], core_ids=[0]).results[0]["out"]
```

```python
from contextlib import ExitStack

import concourse.bass as bass
from concourse import mybir

F32 = mybir.dt.float32
F32R = mybir.dt.float32r
I32 = mybir.dt.int32
ALU = mybir.AluOpType
ACT = mybir.ActivationFunctionType

B = 512
D = 128
TABLES = 26
NF = TABLES + 1
LANES = 128
TILES = B // LANES
Q = 4
QP = 32
U = LANES // Q
LOOKED_UP = [1, 2, 4, 16, 17, 18, 20, 21, 24]
LOOK_FROM = [0, 0, 0, 0, 0, 0, 0, 0, 2]
NL = len(LOOKED_UP)
EARLY = LOOK_FROM.count(0)
GATHERED = [i for i in range(TABLES) if i not in LOOKED_UP]
ORDERED = GATHERED + LOOKED_UP[EARLY:] + LOOKED_UP[:EARLY]
SLOTS = [0] + [i + 1 for i in ORDERED]
NG = len(GATHERED) + NL - EARLY
GROUP = 4


def gathered(t):
    return len(GATHERED) + sum(first > t for first in LOOK_FROM)


GROUPS = [[range(a, min(a + GROUP, gathered(t) + 1)) for a in range(1, gathered(t) + 1, GROUP)]
          for t in range(TILES)]
ROWS = 1000
KP = 125
KC = ROWS // KP
HALF = KC // 2
DELTAS = NF // 2
ZG = 9
ZC = NF // ZG
ZK = ZG * DELTAS
H1, H2 = 512, 256
M1, M2 = H1 // 128, H2 // 128
GM = (Q - 1) * QP + NF
UNIT = 8
UNITS = U // UNIT
BANKS = 4
WARM_UP = 12
OH_RING = 3
HL_RING = 2
RAW_RING = 3


def slot_of(j):
    return 1 + ORDERED.index(LOOKED_UP[j])


def turns_until(t, g):
    return sum(len(GROUPS[x]) for x in range(t)) + g + 1


def work_order():
    turns = [("turn", t, g) for t in range(TILES) for g in range(len(GROUPS[t]))]
    order = []

    def turn(t, leave):
        while turns and turns[0][1] <= t and sum(x[1] <= t for x in turns) > leave:
            order.append(turns.pop(0))

    for j in range(EARLY):
        order += [("compare", j, 0), ("look", j, 0)]
        if j:
            order.append(turns.pop(0))
    order.append(turns.pop(0))

    turn(0, 0)
    order.append(("gram", 0, 0))
    turn(1, 0)
    order += [("compare", j, 0) for j in range(EARLY, NL)]
    order.append(("gram", 0, 1))
    order += [("look", j, 0) for j in range(EARLY, NL)]
    order += [("gram", 1, 0), ("pairs", 0, 0), ("gram", 1, 1), ("l1", 0, 0), ("l1", 0, 1)]
    turn(2, 2)
    order += [("l2", 0, 0), ("l2", 0, 1)]
    turn(2, 0)
    order += [("l3", 0, 0), ("pairs", 1, 0), ("gram", 2, 0), ("gram", 2, 1), ("l1", 1, 0), ("l1", 1, 1)]
    turn(3, 2)
    order += [("l2", 1, 0), ("l2", 1, 1), ("pairs", 2, 0)]
    turn(3, 1)
    order.append(("l1", 2, 0))
    turn(3, 0)
    order += [("l3", 1, 0), ("gram", 3, 0), ("gram", 3, 1), ("l1", 2, 1), ("l2", 2, 0), ("pairs", 3, 0),
              ("l2", 2, 1), ("l1", 3, 0), ("l1", 3, 1), ("l3", 2, 0), ("l2", 3, 0), ("l2", 3, 1), ("l3", 3, 0)]
    return order


ORDER = work_order()

USES = [use for use in ORDER if use[0] not in ("compare", "gram")]


def bank(step, i, part=0):
    return USES.index((step, i, part)) % BANKS


def tower(nc, bottom, ids, ids_t, tables, w1, b1, w2, b2, w3, out):
    ctx = ExitStack()
    with ctx:
        def sb(name, shape, dt=F32):
            return ctx.enter_context(nc.sbuf_tensor(name, shape, dt))

        def sem(name):
            return ctx.enter_context(nc.semaphore(name))

        ids_sb = sb("ids_sb", [128, TILES * TABLES], I32)
        bot = sb("bot", [128, B])
        rows = sb("rows", [128, TILES, NG, D])
        emb = sb("emb", [128, TILES, LANES, QP])
        gram = sb("gram", [128, 2, NF, U])
        pairs = sb("pairs", [128, NF - 1 + DELTAS, QP])
        z = sb("z", [128, NF * DELTAS])
        zt = sb("zt", [ZK, 2, ZC, LANES])
        h1 = sb("h1", [128, 2, M1, LANES])
        h2 = sb("h2", [128, 2, M2, LANES])
        y = sb("y", [1, B])
        raw = sb("raw", [KP, RAW_RING, KC * D])
        hi = sb("hi", [KP, HL_RING, KC * D], F32R)
        lo = sb("lo", [KP, HL_RING, KC * D], F32R)
        ids_b = sb("ids_b", [KP, HL_RING, B], I32)
        ids_f = sb("ids_f", [KP, HL_RING, B])
        onehot = sb("onehot", [KP, OH_RING, HALF, B], F32R)
        first_i = sb("first_i", [KP, 1], I32)
        first_f = sb("first_f", [KP, 1])
        ident = sb("ident", [128, 128])
        w1z = sb("w1z", [ZK, ZC, H1])
        w1b = sb("w1b", [128, H1])
        w2_sb = sb("w2_sb", [128, M1, H2])
        w3_sb = sb("w3_sb", [128, M2])
        b1_sb = sb("b1_sb", [128, M1])
        b2_sb = sb("b2_sb", [128, M2])

        ring = ctx.enter_context(nc.psum_tensor("ring", [128, BANKS, 512], F32))
        gps = ctx.enter_context(nc.psum_tensor("gps", [128, 2, UNIT, 128], F32))

        ids_in = sem("ids_in")
        bot_in = sem("bot_in")
        w_in = sem("w_in")
        raw_in = [sem(f"raw_in{k}") for k in range(RAW_RING)]
        first_raw_in = sem("first_raw_in")
        idb_in = [sem(f"idb_in{j}") for j in range(NL)]
        rows_in = [[sem(f"rows_in{t}_{g}") for g in range(len(GROUPS[t]))] for t in range(TILES)]
        out_done = sem("out_done")
        ident_set = sem("ident_set")
        blank_set = sem("blank_set")
        ones_set = sem("ones_set")
        pad_set = sem("pad_set")
        row_set = sem("row_set")
        row_ready = sem("row_ready")
        idf_ready = sem("idf_ready")
        hi_ready = sem("hi_ready")
        lo_ready = sem("lo_ready")
        oh_ready = sem("oh_ready")
        oh_used = sem("oh_used")
        turned = sem("turned")
        emb_look = sem("emb_look")
        emb_bot = sem("emb_bot")
        emb_turned = sem("emb_turned")
        gram_done = sem("gram_done")
        cut_act = sem("cut_act")
        cut_dve = sem("cut_dve")
        pairs_ready = sem("pairs_ready")
        z_ready = sem("z_ready")
        pairs_done = sem("pairs_done")
        zt_ready = sem("zt_ready")
        l1_done = sem("l1_done")
        h1_act = sem("h1_act")
        h1_dve = sem("h1_dve")
        l2_done = sem("l2_done")
        h2_act = sem("h2_act")
        h2_dve = sem("h2_dve")
        l3_done = sem("l3_done")
        y_ready = sem("y_ready")

        def emb_slots(t, first, count):
            return emb[:, t, :, first:first + count].rearrange("d p f -> d f p")

        block = ctx.enter_context(nc.Block())

        @block.sync
        def _(sp):
            sp.dma_start(ids_sb[:], ids.rearrange("(p t) f -> p (t f)", t=TILES)).then_inc(ids_in, 16)

            def load_ids(j):
                if j >= HL_RING:
                    sp.wait_ge(idf_ready, j - HL_RING + 1)
                row = ids_t[LOOKED_UP[j]:LOOKED_UP[j] + 1, :]
                sp.dma_start(ids_b[:, j % HL_RING, :], row.broadcast_to([KP, B])).then_inc(idb_in[j], 16)

            for j in range(NL):
                load_ids(j)
                if j >= RAW_RING:
                    sp.wait_ge(lo_ready, 2 * (j - RAW_RING + 1))
                table = tables[LOOKED_UP[j]].rearrange("(p k) d -> p (k d)", k=KC)
                start = 0
                if j == 0:
                    sp.dma_start(raw[:, 0, 0:HALF * D], table[:, 0:HALF * D]).then_inc(first_raw_in, 16)
                    start = HALF * D
                sp.dma_start(raw[:, j % RAW_RING, start:], table[:, start:]).then_inc(raw_in[j % RAW_RING], 16)
                if j == NL // 2:
                    sp.dma_start(bot[:], bottom).then_inc(bot_in, 16)
            sp.dma_start(w1z[:], w1[0:ZC * ZK, :].rearrange("(c k) n -> k c n", c=ZC)).then_inc(w_in, 16)
            sp.dma_start(w1b[:], w1[ZC * ZK:, :]).then_inc(w_in, 16)
            sp.dma_start(w2_sb[:], w2.rearrange("(c k) n -> k c n", c=M1)).then_inc(w_in, 16)
            sp.dma_start(w3_sb[:], w3).then_inc(w_in, 16)
            sp.dma_start(b1_sb[:], b1).then_inc(w_in, 16)
            sp.dma_start(b2_sb[:], b2).then_inc(w_in, 16)
            sp.wait_ge(y_ready, TILES)
            sp.dma_start(out.rearrange("b o -> o b"), y[:]).then_inc(out_done, 16)
            sp.wait_ge(out_done, 16)

        @block.gpsimd
        def _(pool):
            nc.gpsimd.iota(first_i[:], pattern=[[1, 1]], base=0, channel_multiplier=-KC).then_inc(row_set, 1)
            pool.wait_ge(row_set, 1)
            pool.wait_ge(ones_set, 1)
            nc.gpsimd.affine_select(out=ident[:], in_=ident[:], compare_op=ALU.is_equal, fill=0.0, base=0,
                                    pattern=[[-1, 128]], channel_multiplier=1).then_inc(ident_set, 1)
            pool.wait_ge(ident_set, 1)
            nc.gpsimd.memset(gram[QP * (Q - 1):, :, :, :], 0.0).then_inc(blank_set, 1)
            pool.wait_ge(ids_in, 16)

            for t in range(TILES):
                for g, slots in enumerate(GROUPS[t]):
                    for slot in slots:
                        table = ORDERED[slot - 1]
                        col = t * TABLES + table
                        nc.gpsimd.indirect_dma_start(
                            out=rows[:, t, slot - 1, :], out_offset=None, in_=tables[table],
                            in_offset=bass.IndirectOffsetOnAxis(ap=ids_sb[:, col:col + 1], axis=0),
                        ).then_inc(rows_in[t][g], 16)

        @block.scalar
        def _(act):
            def float_ids(j):
                act.wait_ge(idb_in[j], 16)
                if j >= HL_RING:
                    act.wait_ge(oh_ready, 2 * (j - HL_RING + 1))
                if j == 0:
                    act.wait_ge(row_ready, 1)
                nc.scalar.activation(ids_f[:, j % HL_RING, :], ids_b[:, j % HL_RING, :], ACT.Identity,
                                     bias=first_f[:]).then_inc(idf_ready, 1)

            def split(j):
                start, halves = 0, 2
                if j == 0:
                    act.wait_ge(first_raw_in, 16)
                    nc.scalar.copy(hi[:, 0, 0:HALF * D], raw[:, 0, 0:HALF * D]).then_inc(hi_ready, 1)
                    start, halves = HALF * D, 1
                act.wait_ge(raw_in[j % RAW_RING], 16 * (j // RAW_RING + 1))
                if j >= HL_RING:
                    act.wait_ge(oh_used, 2 * (j - HL_RING + 1))
                nc.scalar.copy(hi[:, j % HL_RING, start:], raw[:, j % RAW_RING, start:]).then_inc(hi_ready, halves)

            for step, t, part in ORDER:
                if step == "compare":
                    if t == 0:
                        for j in range(HL_RING):
                            float_ids(j)
                            split(j)
                elif step == "look":
                    if t and t + 1 < NL:
                        float_ids(t + 1)
                        split(t + 1)
                    act.wait_ge(oh_used, 2 * (t + 1))
                    first = LOOK_FROM[t]
                    n = TILES - first
                    nc.scalar.copy(emb[:, first:, :, slot_of(t)],
                                   ring[:, bank(step, t), 0:n * LANES].rearrange("d (p t) -> d t p", t=n)
                                   ).then_inc(emb_look, 1)
                    if t == EARLY - 2:
                        act.wait_ge(bot_in, 16)
                        nc.scalar.copy(emb[:, :, :, 0], bot[:].rearrange("d (p t) -> d t p", t=TILES)
                                       ).then_inc(emb_bot, 1)
                elif step == "turn":
                    act.wait_ge(turned, turns_until(t, part))
                    b = bank(step, t, part)
                    slots = GROUPS[t][part]
                    n = len(slots)
                    nc.scalar.copy(emb_slots(t, slots[0], n),
                                   ring[:, b, 0:n * LANES].rearrange("d (f p) -> d f p", f=n)
                                   ).then_inc(emb_turned, 1)
                elif step == "gram":
                    if t == 0:
                        act.wait_ge(blank_set, 1)
                    if t >= 2:
                        act.wait_ge(pairs_ready, 2 * (t - 1))
                    for n in range(part * UNITS // 2, (part + 1) * UNITS // 2):
                        act.wait_ge(gram_done, t * UNITS + n + 1)
                        for q in (2, 3):
                            ins = nc.scalar.copy(
                                gram[QP * q:min(QP * q + QP, GM), t % 2, :, UNIT * n:UNIT * n + UNIT]
                                .rearrange("g f u -> g u f"),
                                gps[QP * q:min(QP * q + QP, GM), n % 2, :, NF * q:NF * q + NF])
                        ins.then_inc(cut_act, 1)
                elif step == "pairs":
                    if t >= 2:
                        act.wait_ge(l1_done, 2 * (t - 1))
                    act.wait_ge(pairs_done, t + 1)
                    b = bank(step, t)
                    nc.scalar.copy(zt[:, t % 2, :, :], ring[0:ZK, b, 0:ZC * LANES].rearrange("k (c p) -> k c p", c=ZC)
                                   ).then_inc(zt_ready, 1)
                elif step == "l1":
                    if t == 0:
                        act.wait_ge(w_in, 16 * 6)
                    if t >= 2:
                        act.wait_ge(l2_done, M2 * (t - 1))
                    if part == 0:
                        continue
                    b = bank(step, t, 1)
                    act.wait_ge(l1_done, 2 * t + 2)
                    for n in range(M1 // 2):
                        m = M1 // 2 + n
                        nc.scalar.activation(h1[:, t % 2, m, :], ring[:, b, n * LANES:(n + 1) * LANES], ACT.Relu,
                                             bias=b1_sb[:, m:m + 1]).then_inc(h1_act, 1)
                elif step == "l2":
                    if t >= 2:
                        act.wait_ge(l3_done, t - 1)
                    if part == 1:
                        continue
                    b = bank(step, t, 0)
                    act.wait_ge(l2_done, M2 * t + 1)
                    nc.scalar.activation(h2[:, t % 2, 0, :], ring[:, b, 0:LANES], ACT.Relu,
                                         bias=b2_sb[:, 0:1]).then_inc(h2_act, 1)
                elif step == "l3":
                    b = bank(step, t)
                    act.wait_ge(l3_done, t + 1)
                    nc.scalar.copy(y[0:1, :].rearrange("o (u q t) -> o q u t", q=Q, t=TILES)[:, :, :, t],
                                   ring[0:1, b, 0:LANES].rearrange("o (q u) -> o q u", q=Q)
                                   ).then_inc(y_ready, 1)

        @block.vector
        def _(dve):
            nc.vector.memset(ident[:], 1.0).then_inc(ones_set, 1)
            dve.wait_ge(row_set, 1)
            nc.vector.tensor_copy(first_f[:], first_i[:]).then_inc(row_ready, 1)
            nc.vector.memset(emb[:, :, :, NF:QP], 0.0).then_inc(pad_set, 1)

            for step, t, part in ORDER:
                if step == "compare":
                    dve.wait_ge(idf_ready, t + 1)
                    first = LOOK_FROM[t]
                    numbers = ids_f[:, t % HL_RING, :].rearrange("r (p t) -> r p t", t=TILES)[:, :, first:]
                    width = LANES * (TILES - first)
                    for half in range(2):
                        n = 2 * t + half
                        if n >= OH_RING:
                            dve.wait_ge(oh_used, n - OH_RING + 1)
                        for k in range(HALF):
                            chunk = HALF * half + k
                            out_k = onehot[:, n % OH_RING, k, 0:width].rearrange("r (p t) -> r p t", p=LANES)
                            ins = nc.vector.tensor_scalar(out_k, numbers,
                                                          float(chunk), None, ALU.is_equal)
                        ins.then_inc(oh_ready, 1)
                        if half == 0 or t == 0:
                            start, end = (half * HALF * D, (half + 1) * HALF * D) if t == 0 else (0, KC * D)
                            halves = 1 if t == 0 else 2
                            dve.wait_ge(hi_ready, 2 * t + (half + 1 if t == 0 else 2))
                            if t >= HL_RING:
                                dve.wait_ge(oh_used, 2 * (t - HL_RING + 1))
                            nc.vector.tensor_tensor(lo[:, t % HL_RING, start:end], raw[:, t % RAW_RING, start:end],
                                                    hi[:, t % HL_RING, start:end].bitcast(F32),
                                                    ALU.subtract).then_inc(lo_ready, halves)
                elif step == "gram":
                    if t >= 2:
                        dve.wait_ge(pairs_ready, 2 * (t - 1))
                    for n in range(part * UNITS // 2, (part + 1) * UNITS // 2):
                        dve.wait_ge(gram_done, t * UNITS + n + 1)
                        for q in (0, 1):
                            ins = nc.vector.tensor_copy(
                                gram[QP * q:QP * q + QP, t % 2, :, UNIT * n:UNIT * n + UNIT]
                                .rearrange("g f u -> g u f"),
                                gps[QP * q:QP * q + QP, n % 2, :, NF * q:NF * q + NF])
                        ins.then_inc(cut_dve, 1)
                    if part == 0:
                        continue
                    dve.wait_ge(cut_dve, UNITS * (t + 1))
                    dve.wait_ge(cut_act, UNITS * (t + 1))
                    if t:
                        dve.wait_ge(z_ready, t)
                    nc.vector.transpose(pairs[:, 0:NF - 1, :], gram[:, t % 2, 1:NF, :]).then_inc(pairs_ready, 1)
                    nc.vector.transpose(pairs[:, NF - 1:, :], gram[:, t % 2, 0:DELTAS, :]).then_inc(pairs_ready, 1)
                    dve.wait_ge(pairs_ready, 2 * (t + 1))
                    if t:
                        dve.wait_ge(pairs_done, t)
                    start = pairs[:, 0, 0:1]
                    picked = bass.AP(start.tensor, start.offset, [list(start.ap[0]), [QP + 1, NF], [QP, DELTAS]])
                    nc.vector.tensor_copy(z[:].rearrange("p (g e) -> p g e", g=NF), picked).then_inc(z_ready, 1)
                elif step == "l1":
                    if t == 0:
                        dve.wait_ge(w_in, 16 * 6)
                    if t >= 2:
                        dve.wait_ge(l2_done, M2 * (t - 1))
                    if part == 1:
                        continue
                    b = bank(step, t, 0)
                    dve.wait_ge(l1_done, 2 * t + 1)
                    for m in range(M1 // 2):
                        nc.vector.tensor_scalar(h1[:, t % 2, m, :], ring[:, b, m * LANES:(m + 1) * LANES],
                                                b1_sb[:, m:m + 1], 0.0, ALU.add, ALU.max).then_inc(h1_dve, 1)
                elif step == "l2":
                    if t >= 2:
                        dve.wait_ge(l3_done, t - 1)
                    if part == 0:
                        continue
                    b = bank(step, t, 1)
                    dve.wait_ge(l2_done, M2 * t + 2)
                    nc.vector.tensor_scalar(h2[:, t % 2, 1, :], ring[:, b, 0:LANES],
                                            b2_sb[:, 1:2], 0.0, ALU.add, ALU.max).then_inc(h2_dve, 1)

        @block.tensor
        def _(pe):
            def wait_emptied(step, t, part=0):
                n = USES.index((step, t, part))
                if n < BANKS:
                    return
                was, i, g = USES[n - BANKS]
                if was == "look":
                    pe.wait_ge(emb_look, i + 1)
                elif was == "turn":
                    pe.wait_ge(emb_turned, turns_until(i, g))
                elif was == "pairs":
                    pe.wait_ge(zt_ready, i + 1)
                elif was == "l1":
                    pe.wait_ge(h1_act if g else h1_dve, M1 // 2 * (i + 1))
                elif was == "l2":
                    pe.wait_ge(h2_dve if g else h2_act, i + 1)
                elif was == "l3":
                    pe.wait_ge(y_ready, i + 1)

            pe.wait_ge(ident_set, 1)
            for n in range(WARM_UP):
                nc.tensor.matmul(gps[:, 0, 0, :], ident[:], ident[:], start=True, stop=True)

            for step, t, part in ORDER:
                b = bank(step, t, part) if step not in ("gram", "compare") else None
                if step == "look":
                    wait_emptied(step, t)
                    width = LANES * (TILES - LOOK_FROM[t])
                    for half in range(2):
                        n = 2 * t + half
                        pe.wait_ge(oh_ready, n + 1)
                        pe.wait_ge(hi_ready, n + 1)
                        for part_of in (hi, lo):
                            if part_of is lo:
                                pe.wait_ge(lo_ready, n + 1)
                            for k in range(HALF):
                                chunk = HALF * half + k
                                mm = nc.tensor.matmul(ring[:, b, 0:width],
                                                      part_of[:, t % HL_RING, chunk * D:(chunk + 1) * D],
                                                      onehot[:, n % OH_RING, k, 0:width],
                                                      start=(chunk == 0 and part_of is hi),
                                                      stop=(chunk == KC - 1 and part_of is lo))
                        mm.then_inc(oh_used, 1)
                elif step == "turn":
                    wait_emptied(step, t, part)
                    slots = GROUPS[t][part]
                    pe.wait_ge(rows_in[t][part], 16 * len(slots))
                    for n, slot in enumerate(slots):
                        mm = nc.tensor.transpose(ring[:, b, n * LANES:(n + 1) * LANES], rows[:, t, slot - 1, :],
                                                 ident[:])
                    mm.then_inc(turned, 1)
                elif step == "gram":
                    if t == 0:
                        pe.wait_ge(emb_bot, 1)
                        pe.wait_ge(emb_look, EARLY)
                        pe.wait_ge(pad_set, 1)
                    if EARLY < NL and t == LOOK_FROM[-1]:
                        pe.wait_ge(emb_look, NL)
                    pe.wait_ge(emb_turned, turns_until(t, len(GROUPS[t]) - 1))
                    for n in range(part * UNITS // 2, (part + 1) * UNITS // 2):
                        unit = t * UNITS + n
                        if unit >= 2:
                            pe.wait_ge(cut_act, unit - 1)
                            pe.wait_ge(cut_dve, unit - 1)
                        for k in range(UNIT):
                            four = emb[:, t, Q * (UNIT * n + k):Q * (UNIT * n + k + 1), :]
                            mm = nc.tensor.matmul(gps[0:GM, n % 2, k, 0:Q * NF],
                                                  four.rearrange("d q f -> d (q f)")[:, 0:GM],
                                                  four[:, :, 0:NF], start=True, stop=True)
                        mm.then_inc(gram_done, 1)
                elif step == "pairs":
                    wait_emptied(step, t)
                    pe.wait_ge(z_ready, t + 1)
                    for c in range(ZC):
                        mm = nc.tensor.transpose(ring[0:ZK, b, c * LANES:(c + 1) * LANES],
                                                 z[:, c * ZK:(c + 1) * ZK], ident[:])
                    mm.then_inc(pairs_done, 1)
                elif step == "l1":
                    if t == 0:
                        pe.wait_ge(w_in, 16 * 6)
                    pe.wait_ge(zt_ready, t + 1)
                    wait_emptied(step, t, part)
                    for n in range(M1 // 2):
                        m = part * M1 // 2 + n
                        o = ring[:, b, n * LANES:(n + 1) * LANES]
                        nc.tensor.matmul(o, w1b[:, m * 128:(m + 1) * 128],
                                         emb[:, t, :, 0].rearrange("d (u q) -> d q u", q=Q),
                                         start=True, stop=False)
                        for c in range(ZC):
                            mm = nc.tensor.matmul(o, w1z[:, c, m * 128:(m + 1) * 128], zt[:, t % 2, c, :],
                                                  start=False, stop=(c == ZC - 1))
                    mm.then_inc(l1_done, 1)
                elif step == "l2":
                    wait_emptied(step, t, part)
                    for k in range(M1):
                        half, n = divmod(k, M1 // 2)
                        if part == 0:
                            pe.wait_ge(h1_act if half else h1_dve, M1 // 2 * t + n + 1)
                        mm = nc.tensor.matmul(ring[:, b, 0:LANES], w2_sb[:, k, part * 128:(part + 1) * 128],
                                              h1[:, t % 2, k, :], start=(k == 0), stop=(k == M1 - 1))
                    mm.then_inc(l2_done, 1)
                elif step == "l3":
                    wait_emptied(step, t)
                    for k in range(M2):
                        pe.wait_ge(h2_dve if k % 2 else h2_act, t + 1)
                        mm = nc.tensor.matmul(ring[0:1, b, 0:LANES], w3_sb[:, k:k + 1], h2[:, t % 2, k, :],
                                              start=(k == 0), stop=(k == M2 - 1))
                    mm.then_inc(l3_done, 1)


def pair_rows():
    rows = []
    for g in range(NF):
        for delta in range(1, DELTAS + 1):
            i, j = sorted((SLOTS[g], SLOTS[(g + delta) % NF]))
            rows.append(i * (2 * NF - i - 1) // 2 + j - i - 1)
    return rows


def kernel(**inputs):
    import numpy as np
    import concourse.bacc as bacc
    from concourse.bass_utils import run_bass_kernel_spmd

    nc = bacc.Bacc("TRN2", target_bir_lowering=False, num_devices=1)
    arrays = {}

    def given(name, array):
        array = np.ascontiguousarray(array)
        arrays[name] = array
        return nc.dram_tensor(name, array.shape, mybir.dt.from_np(array.dtype), kind="ExternalInput").ap()

    w1 = np.asarray(inputs["W_top1"])
    order = pair_rows() + list(range(NF * DELTAS, w1.shape[0]))
    ids = np.asarray(inputs["ids"])
    bottom_d = given("bottom_t", np.asarray(inputs["r_bottom_output"]).T)
    ids_d = given("ids", ids)
    ids_t_d = given("ids_t", ids.T)
    tables_d = [given(f"tbl_{i}", inputs[f"tbl_{i}"]) for i in range(TABLES)]
    w1_d = given("w1", w1[order])
    b1_d = given("b1", np.asarray(inputs["b_top1"]).reshape(M1, 128).T)
    w2_d = given("w2", inputs["W_top2"])
    b2_d = given("b2", np.asarray(inputs["b_top2"]).reshape(M2, 128).T)
    w3_d = given("w3", np.asarray(inputs["W_top3"]).reshape(M2, 128).T)
    out_d = nc.dram_tensor("out", (B, 1), F32, kind="ExternalOutput").ap()
    tower(nc, bottom_d, ids_d, ids_t_d, tables_d, w1_d, b1_d, w2_d, b2_d, w3_d, out_d)
    return run_bass_kernel_spmd(nc, [arrays], core_ids=[0]).results[0]["out"]
```
